# Optimizing a Trainium2 kernel written in Bass

```python
import numpy as np
import jax
import jax.numpy as jnp

def _softmax(x, axis=-1):
    return jax.nn.softmax(x, axis=axis)
def _gelu(x):
    return jax.nn.gelu(x, approximate=True)
def _silu(x):
    return jax.nn.silu(x)
def _sigmoid(x):
    return jax.nn.sigmoid(x)
def _layernorm(x, axis=-1, eps=1e-5):
    m = jnp.mean(x, axis=axis, keepdims=True)
    v = jnp.var(x, axis=axis, keepdims=True)
    return (x - m) / jnp.sqrt(v + eps)
def _scatter_add(tgt, idx, src, axis=0):
    return tgt.at[idx].add(src)
def _segment_sum(src, seg, n):
    return jax.ops.segment_sum(src, seg, n)

kernel_name = 'mk_metaformer_d1_conv_nchw512_582b3a'

def setup_inputs(seed: int = 0):
    np.random.seed(seed)
    _w = jnp.asarray
    def _rec_inputs():
        import jax
        import jax.numpy as jnp
        _gk = jax.random.key(seed)
        x = -0.0003929 + 0.9999 * jax.random.normal(jax.random.fold_in(_gk, 1), (8, 512, 64, 64), jnp.float32)
        return x
    x = _rec_inputs()
    def _L0_conv_setup():
        import jax, jax.numpy as jnp
        from jax import lax
        import numpy as np
        UP = 2
        DOWN = 2
        PADDING = (11, 10, 11, 10)
        GAIN = float(np.sqrt(2.0))
        SLOPE = 0.2
        CLAMP = 256.0
        UP_TAPS = 12
        IN_CUTOFF = 8.0
        OUT_CUTOFF = 8.0
        IN_HALF_WIDTH = 6.0
        OUT_HALF_WIDTH = 6.0
        TEMP_FS = 32.0

        def _design_lowpass(numtaps, cutoff, width, fs):
            nyq = fs / 2.0
            atten = 2.285 * (numtaps - 1) * np.pi * (width / nyq) + 7.95
            if atten > 50.0:
                beta = 0.1102 * (atten - 8.7)
            elif atten > 21.0:
                beta = 0.5842 * (atten - 21.0) ** 0.4 + 0.07886 * (atten - 21.0)
            else:
                beta = 0.0
            m = np.arange(numtaps) - (numtaps - 1) / 2.0
            c = cutoff / nyq
            h = c * np.sinc(c * m)
            h = h * np.kaiser(numtaps, beta)
            h = h / np.sum(h)
            return h.astype(np.float32)

        def _upfirdn2d_sep(x, f, up, down, pad, gain):
            N, C, H, W = x.shape
            fr = f[::-1].astype(x.dtype)
            kH = fr.reshape(1, 1, -1, 1)
            kW = fr.reshape(1, 1, 1, -1)
            px0, px1, py0, py1 = pad
            xr = x.reshape(N * C, 1, H, W)
            xr = lax.conv_general_dilated(xr, kH, window_strides=(down, 1), padding=((py0, py1 + up - 1), (0, 0)), lhs_dilation=(up, 1))
            xr = lax.conv_general_dilated(xr, kW, window_strides=(1, down), padding=((0, 0), (px0, px1 + up - 1)), lhs_dilation=(1, up))
            Ho, Wo = (xr.shape[2], xr.shape[3])
            return xr.reshape(N, C, Ho, Wo) * gain
        key = jax.random.key(seed)
        k1, k2 = jax.random.split(key)
        x = jax.random.normal(k1, (8, 512, 64, 64), dtype=jnp.float32)
        bias = jax.random.normal(k2, (512,), dtype=jnp.float32) * 0.1
        up_filter = jnp.asarray(_design_lowpass(UP_TAPS, IN_CUTOFF, IN_HALF_WIDTH * 2, TEMP_FS))
        down_filter = jnp.asarray(_design_lowpass(UP_TAPS, OUT_CUTOFF, OUT_HALF_WIDTH * 2, TEMP_FS))
        return {'x': x, 'bias': bias, 'up_filter': up_filter, 'down_filter': down_filter}
    _L0_conv_all = _L0_conv_setup()
    _L0_conv_in = {k: v for k, v in _L0_conv_all.items() if k in ('bias', 'up_filter', 'down_filter', )}
    del _L0_conv_all

    def _L0_ffn_setup():
        import jax, jax.numpy as jnp
        import numpy as np
        DIM = 512
        MOE_DIM = 256
        E = 64
        G = 8
        TOPK_G = 4
        K = 8
        SCALE = 2.5
        CAP = 1024

        def _gate(x2, gate_w, gate_b):
            T = x2.shape[0]
            scores = jax.nn.sigmoid(x2 @ gate_w.T)
            s = (scores + gate_b).reshape(T, G, E // G)
            group_scores = jax.lax.top_k(s, 2)[0].sum(-1)
            top_groups = jax.lax.top_k(group_scores, TOPK_G)[1]
            gmask = jnp.zeros((T, G), bool).at[jnp.arange(T)[:, None], top_groups].set(True)
            s = jnp.where(gmask[..., None], s, -jnp.inf).reshape(T, E)
            idx = jax.lax.top_k(s, K)[1]
            w = jnp.take_along_axis(scores, idx, axis=1)
            w = w / w.sum(-1, keepdims=True) * SCALE
            return (w, idx)

        def _moe_forward(x, gate_w, gate_b, w1, w3, w2):
            shape = x.shape
            x2 = x.reshape(-1, DIM)
            T = x2.shape[0]
            w, idx = _gate(x2, gate_w, gate_b)
            flat_e = idx.reshape(-1)
            oh = (flat_e[:, None] == jnp.arange(E)[None, :]).astype(jnp.int32)
            pos = (jnp.cumsum(oh, axis=0) * oh).sum(-1) - 1
            x_rep = jnp.repeat(x2, K, axis=0)
            xb = jnp.zeros((E, CAP, DIM), x2.dtype).at[flat_e, pos].set(x_rep, mode='drop')
            h = jax.nn.silu(jnp.einsum('ecd,edm->ecm', xb, w1)) * jnp.einsum('ecd,edm->ecm', xb, w3)
            yb = jnp.einsum('ecm,emd->ecd', h, w2)
            y = yb.at[flat_e, pos].get(mode='fill', fill_value=0.0) * w.reshape(-1)[:, None]
            return y.reshape(T, K, DIM).sum(1).reshape(shape)
        key = jax.random.key(seed)
        ks = jax.random.split(key, 6)
        x = jax.random.normal(ks[0], (4, 512, DIM), jnp.float32)
        gate_w = jax.random.normal(ks[1], (E, DIM), jnp.float32) / np.sqrt(DIM).astype(np.float32)
        gate_b = jax.random.normal(ks[2], (E,), jnp.float32) * 0.01
        w1 = jax.random.normal(ks[3], (E, DIM, MOE_DIM), jnp.float32) / np.sqrt(DIM).astype(np.float32)
        w3 = jax.random.normal(ks[4], (E, DIM, MOE_DIM), jnp.float32) / np.sqrt(DIM).astype(np.float32)
        w2 = jax.random.normal(ks[5], (E, MOE_DIM, DIM), jnp.float32) / np.sqrt(MOE_DIM).astype(np.float32)
        return {'x': x, 'gate_w': gate_w, 'gate_b': gate_b, 'w1': w1, 'w3': w3, 'w2': w2}
    _L0_ffn_all = _L0_ffn_setup()
    _L0_ffn_in = {k: v for k, v in _L0_ffn_all.items() if k in ('gate_w', 'gate_b', 'w1', 'w3', 'w2', )}
    del _L0_ffn_all

    return {
        "x": x,
        "L0_conv_bias": _L0_conv_in["bias"],
        "L0_conv_up_filter": _L0_conv_in["up_filter"],
        "L0_conv_down_filter": _L0_conv_in["down_filter"],
        "L0_ffn_gate_w": _L0_ffn_in["gate_w"],
        "L0_ffn_gate_b": _L0_ffn_in["gate_b"],
        "L0_ffn_w1": _L0_ffn_in["w1"],
        "L0_ffn_w3": _L0_ffn_in["w3"],
        "L0_ffn_w2": _L0_ffn_in["w2"],
    }

def reference(x, L0_conv_bias, L0_conv_up_filter, L0_conv_down_filter, L0_ffn_gate_w, L0_ffn_gate_b, L0_ffn_w1, L0_ffn_w3, L0_ffn_w2):
    import jax
    import jax.numpy as jnp
    def _L0_conv_ref(x, bias, up_filter, down_filter):
        import jax, jax.numpy as jnp
        from jax import lax
        import numpy as np
        UP = 2
        DOWN = 2
        PADDING = (11, 10, 11, 10)
        GAIN = float(np.sqrt(2.0))
        SLOPE = 0.2
        CLAMP = 256.0
        UP_TAPS = 12
        IN_CUTOFF = 8.0
        OUT_CUTOFF = 8.0
        IN_HALF_WIDTH = 6.0
        OUT_HALF_WIDTH = 6.0
        TEMP_FS = 32.0

        def _design_lowpass(numtaps, cutoff, width, fs):
            nyq = fs / 2.0
            atten = 2.285 * (numtaps - 1) * np.pi * (width / nyq) + 7.95
            if atten > 50.0:
                beta = 0.1102 * (atten - 8.7)
            elif atten > 21.0:
                beta = 0.5842 * (atten - 21.0) ** 0.4 + 0.07886 * (atten - 21.0)
            else:
                beta = 0.0
            m = np.arange(numtaps) - (numtaps - 1) / 2.0
            c = cutoff / nyq
            h = c * np.sinc(c * m)
            h = h * np.kaiser(numtaps, beta)
            h = h / np.sum(h)
            return h.astype(np.float32)

        def _upfirdn2d_sep(x, f, up, down, pad, gain):
            N, C, H, W = x.shape
            fr = f[::-1].astype(x.dtype)
            kH = fr.reshape(1, 1, -1, 1)
            kW = fr.reshape(1, 1, 1, -1)
            px0, px1, py0, py1 = pad
            xr = x.reshape(N * C, 1, H, W)
            xr = lax.conv_general_dilated(xr, kH, window_strides=(down, 1), padding=((py0, py1 + up - 1), (0, 0)), lhs_dilation=(up, 1))
            xr = lax.conv_general_dilated(xr, kW, window_strides=(1, down), padding=((0, 0), (px0, px1 + up - 1)), lhs_dilation=(1, up))
            Ho, Wo = (xr.shape[2], xr.shape[3])
            return xr.reshape(N, C, Ho, Wo) * gain
        y = _upfirdn2d_sep(x, up_filter, UP, 1, PADDING, float(UP * UP))
        y = y + bias[None, :, None, None]
        y = jnp.where(y >= 0, y, y * SLOPE) * GAIN
        y = jnp.clip(y, -CLAMP, CLAMP)
        y = _upfirdn2d_sep(y, down_filter, 1, DOWN, (0, 0, 0, 0), 1.0)
        return y

    def _L0_ffn_ref(x, gate_w, gate_b, w1, w3, w2):
        import jax, jax.numpy as jnp
        import numpy as np
        DIM = 512
        MOE_DIM = 256
        E = 64
        G = 8
        TOPK_G = 4
        K = 8
        SCALE = 2.5
        CAP = 1024

        def _gate(x2, gate_w, gate_b):
            T = x2.shape[0]
            scores = jax.nn.sigmoid(x2 @ gate_w.T)
            s = (scores + gate_b).reshape(T, G, E // G)
            group_scores = jax.lax.top_k(s, 2)[0].sum(-1)
            top_groups = jax.lax.top_k(group_scores, TOPK_G)[1]
            gmask = jnp.zeros((T, G), bool).at[jnp.arange(T)[:, None], top_groups].set(True)
            s = jnp.where(gmask[..., None], s, -jnp.inf).reshape(T, E)
            idx = jax.lax.top_k(s, K)[1]
            w = jnp.take_along_axis(scores, idx, axis=1)
            w = w / w.sum(-1, keepdims=True) * SCALE
            return (w, idx)

        def _moe_forward(x, gate_w, gate_b, w1, w3, w2):
            shape = x.shape
            x2 = x.reshape(-1, DIM)
            T = x2.shape[0]
            w, idx = _gate(x2, gate_w, gate_b)
            flat_e = idx.reshape(-1)
            oh = (flat_e[:, None] == jnp.arange(E)[None, :]).astype(jnp.int32)
            pos = (jnp.cumsum(oh, axis=0) * oh).sum(-1) - 1
            x_rep = jnp.repeat(x2, K, axis=0)
            xb = jnp.zeros((E, CAP, DIM), x2.dtype).at[flat_e, pos].set(x_rep, mode='drop')
            h = jax.nn.silu(jnp.einsum('ecd,edm->ecm', xb, w1)) * jnp.einsum('ecd,edm->ecm', xb, w3)
            yb = jnp.einsum('ecm,emd->ecd', h, w2)
            y = yb.at[flat_e, pos].get(mode='fill', fill_value=0.0) * w.reshape(-1)[:, None]
            return y.reshape(T, K, DIM).sum(1).reshape(shape)
        return _moe_forward(x, gate_w, gate_b, w1, w3, w2)

    def _gn(v, G=32, eps=1e-5):
        B_, C_, H_, W_ = v.shape
        g = v.reshape(B_, G, C_ // G, H_, W_)
        m = jnp.mean(g, axis=(2, 3, 4), keepdims=True)
        s = jnp.var(g, axis=(2, 3, 4), keepdims=True)
        return ((g - m) / jnp.sqrt(s + eps)).reshape(v.shape)

    def _ln_c(v, eps=1e-6):
        m = jnp.mean(v, axis=1, keepdims=True)
        s = jnp.var(v, axis=1, keepdims=True)
        return (v - m) / jnp.sqrt(s + eps)

    def _ln_t(v, eps=1e-5):
        m = jnp.mean(v, axis=-1, keepdims=True)
        s = jnp.var(v, axis=-1, keepdims=True)
        return (v - m) / jnp.sqrt(s + eps)

    def _to_tokens(v):
        B_, C_, H_, W_ = v.shape
        return v.reshape(B_, C_, H_ * W_).transpose(0, 2, 1)
    def _from_tokens(t, like):
        B_, C_, H_, W_ = like.shape
        return t.transpose(0, 2, 1).reshape(B_, C_, H_, W_)

    x = x + _L0_conv_ref(_ln_c(x), L0_conv_bias, L0_conv_up_filter, L0_conv_down_filter)
    t = _to_tokens(x)
    t = t + _L0_ffn_ref(_ln_t(t), L0_ffn_gate_w, L0_ffn_gate_b, L0_ffn_w1, L0_ffn_w3, L0_ffn_w2)
    x = _from_tokens(t, x)
    return x


_drawn_inputs = setup_inputs


def setup_inputs(seed=0):
    import zlib

    import numpy as np

    out = dict(_drawn_inputs(seed))
    spreads = {}
    factors = {}
    for name, (base, spread) in spreads.items():
        noise = np.random.default_rng([zlib.crc32(name.encode()), seed]).standard_normal(out[name].shape)
        drawn = base * np.exp(spread * noise) if base else spread * noise
        out[name] = jnp.asarray(drawn.astype(out[name].dtype))
    for name, factor in factors.items():
        out[name] = (out[name] * factor).astype(out[name].dtype)
    return out
```

```python
import numpy as np

import concourse.bass as bass
import concourse.mybir as mybir

F32 = mybir.dt.float32
F16 = mybir.dt.float16
ALU = mybir.AluOpType
ACT = mybir.ActivationFunctionType
AX = mybir.AxisListType

P = 128
H = W = 64
UP = 138
MAIN = 128
REM = UP - MAIN
REMP = 16
VW = MAIN + REMP
TAPS = 12
TAIL = 5
CG = 8
JG = CG // 2
LN_EPS = 1e-6
CLAMP = 256.0
FILL = 2

def conv_phase(nc, x, bias, bias_cols, consts, out, scratch=()):
    from contextlib import ExitStack
    NI, C = x.shape[0], x.shape[1]
    G = C // CG
    NG = NI * G
    PAIRS = C // 2
    RING = 2 * PAIRS
    x_v = x.rearrange("n (j q) h w -> (n j) (q h) w", q=2)
    out_v = out.rearrange("n (j q) h w -> (n j) (q h) w", q=2)
    CH = 4
    with ExitStack() as ctx:
        def sb(name, shape, dt=F32):
            return ctx.enter_context(nc.sbuf_tensor(name, shape, dt))

        def ps(name, shape):
            return ctx.enter_context(nc.psum_tensor(name, shape, F32))

        def sem(name):
            return ctx.enter_context(nc.semaphore(name))

        cw = {}
        shapes = {k: v.shape[1] for k, v in consts.items()}
        stage = sb("c_stage", [P, max(shapes.values())])
        scaled = sb("c_scaled", [P, max(shapes.values())])
        for k, n in shapes.items():
            cw[k] = [sb(f"c_{k}_{q}", [P, n], F16) for q in ("hi", "lo")]
        up1 = [t[:, 0:2 * VW] for t in cw["up_rows"]]
        up2 = [t[:].rearrange("p (j w) -> p j w", j=2) for t in cw["up_cols"]]
        dn3 = [t[:] for t in cw["down_main"]]
        dn3r = [t[:].rearrange("p (c q) -> p c q", q=TAIL) for t in cw["down_tail_block"]]
        dn3c = [t[:] for t in cw["down_tail_corner"]]
        dn4 = [t[:] for t in cw["down_main_neg"]]
        dn4r = [t[:].rearrange("p (u q) -> p u q", u=2) for t in cw["down_tail_cols"]]
        corner_mask = cw["corner_mask"][0][:]
        ones_rows = cw["bias_ones"][0][:]
        pick_rows = cw["bias_pick"][0][:]
        bias_row = sb("bias_row", [P, C], F16)
        bias_col = sb("bias_col", [P, G], F16)
        b_row = sb("b_row", [P, C])
        b_col = sb("b_col", [P, G])
        average = sb("average", [P, P])

        zeros = sb("zeros", [P, FILL * 576])
        ring = sb("x_ring", [P, RING, W])
        acc_x = sb("acc_x", [P, JG, W])
        acc_sq = sb("acc_sq", [P, JG, W])
        sums = sb("sums", [P, 2, W])
        mom = sb("moments", [P, 2, W])
        std = sb("std", [P, W])
        stats = sb("stats", [P, 2, 2, W])
        sq = sb("sq", [P, 2, JG, W])
        xn = sb("xn", [P, 2, JG, W])
        XD = [sb(f"x16_{q}", [P, 2, JG, W], F16) for q in ("hi", "lo")]
        VD = [sb(f"v16_{q}", [P, 2, 2 * VW, 2], F16) for q in ("hi", "lo")]
        zr = sb("z_relu", [P, 3, 3 * UP])
        zk = sb("z_leaky", [P, 2, 9 * UP])
        ZD = [sb(f"z16_{q}", [P, 2, 9, UP], F16) for q in ("hi", "lo")]
        ZT = [sb(f"zt16_{q}", [P, 2, CG, REM], F16) for q in ("hi", "lo")]
        ZC = [sb(f"zc16_{q}", [P, 2, CG, REM], F16) for q in ("hi", "lo")]
        WD = [sb(f"w16_{q}", [P, 2, CG * H], F16) for q in ("hi", "lo")]
        RD = [sb(f"r16_{q}", [CG * REM, 2, H], F16) for q in ("hi", "lo")]
        ob = sb("out_sb", [P, 2, JG, W])

        v_ps = ps("v_ps", [P, 2, 512])
        z_ps = ps("z_ps", [P, 3, 512])
        w_ps = ps("w_ps", [P, 512])
        r_ps = ps("r_ps", [P, 512])
        o_ps = ps("o_ps", [P, 512])

        s_const, s_cv, s_bias = sem("const_loaded"), sem("const_split"), sem("bias_split")
        s_zero, s_ld = sem("zeroed"), sem("x_loaded")
        s_sq, s_asq, s_ax, s_az = sem("squared"), sem("sq_added"), sem("x_added"), sem("acc_zeroed")
        s_sum, s_mom, s_momr, s_var, s_std, s_stat = (sem("sums_ready"), sem("moments_mm"), sem("moments_read"),
                                                      sem("var_ready"), sem("std_ready"), sem("stats_ready"))
        s_xc, s_xn, s_xh, s_xl = sem("x_centered"), sem("x_normed"), sem("x_hi"), sem("x_lo")
        s_vmm, s_vh, s_vl = sem("v_mm"), sem("v_hi"), sem("v_lo")
        s_zmm, s_zr, s_zk, s_zh, s_zl, s_zc = (sem("z_mm"), sem("z_relu_done"), sem("z_leaky_done"),
                                               sem("z_hi"), sem("z_lo"), sem("z_corner"))
        s_zt, s_clip = sem("z_rest_cols"), sem("z_clipped")
        s_wmm, s_wh, s_wl = sem("w_mm"), sem("w_hi"), sem("w_lo")
        s_omm, s_ob, s_pass = sem("o_mm"), sem("out_ready"), sem("pass")
        s_st, s_fill = [sem("stored_even"), sem("stored_odd")], sem("scratch_zeroed")

        def wait(eng, s, v):
            if not (isinstance(v, int) and v <= 0):
                eng.wait_ge(s, v)

        FIRST = 6
        LAG = 4

        def over_groups(eng, lead, boundary):
            boundary(0)
            for k in range(FIRST):
                lead(k, k % 2, NI > 1)
            with eng.Fori(FIRST // 2, G // 2) as i:
                lead(i * 2, 0, NI > 1)
                lead(i * 2 + 1, 1, NI > 1)
            if NI > 2:
                with eng.Fori(1, NI - 1) as n:
                    boundary(n)
                    with eng.Fori(0, G // 2) as i:
                        lead(n * G + i * 2, 0, True)
                        lead(n * G + i * 2 + 1, 1, True)
            if NI > 1:
                boundary(NI - 1)
                with eng.Fori((NI - 1) * G // 2, NG // 2) as i:
                    lead(i * 2, 0, False)
                    lead(i * 2 + 1, 1, False)
            for k in range(NG, NG + LAG):
                lead(k, k % 2, False)

        def live(k):
            return not isinstance(k, int) or 0 <= k < NG

        def gated(k, lag):
            g = k - lag
            return g, live(g)

        def slot(k):
            return bass.ds((k % (2 * G)) * JG, JG)

        block = ctx.enter_context(nc.Block())

        @block.sync
        def _(sp):
            for i, (k, t) in enumerate(consts.items()):
                wait(sp, s_cv, 3 * i)
                sp.dma_start(stage[:, 0:shapes[k]], t).then_inc(s_const, 16)
            sp.wait_ge(s_zero, 3)
            for r in (0, 32):
                sp.dma_start(b_row[r:r + 1, :], bias.rearrange("(a c) -> a c", a=1)).then_inc(s_bias, 16)
                sp.dma_start(b_col[r:r + CG, :], bias_cols).then_inc(s_bias, 16)

            LPI = G // CH
            LOADS = NI * LPI
            AHEAD = LPI + 1

            def load(m, reused):
                if reused:
                    sp.wait_ge(s_ob, m * CH - 2 * G + CH)
                    sp.sem_inc(s_pass, 1)
                wait(sp, s_ld, m * 16)
                a = m * (CH * JG)
                sp.dma_start(ring[:, bass.ds(a % RING, CH * JG), :],
                             x_v[bass.ds(a, CH * JG)].rearrange("a p w -> p a w")).then_inc(s_ld, 16)

            def zero_rows(c):
                for t in scratch:
                    n = t.shape[1]
                    sp.dma_start(t[bass.ds(c * (P * FILL), P * FILL), :].rearrange("(p a) c -> p (a c)", p=P),
                                 zeros[:, 0:FILL * n]).then_inc(s_fill, 16)

            pieces = [t.shape[0] // (P * FILL) for t in scratch]
            assert all(n >= LOADS for n in pieces)

            def stores(c):
                zero_rows(c)
                for u in range(CH):
                    k = c * CH + u
                    sp.wait_ge(s_ob, k + 1)
                    sp.dma_start(out_v[bass.ds(k * JG, JG)].rearrange("a p w -> p a w"),
                                 ob[:, u % 2]).then_inc(s_st[u % 2], 16)

            for m in range(AHEAD):
                if m < LOADS:
                    load(m, False)
            for c in range(LOADS, max(pieces, default=0)):
                zero_rows(c)
            fresh = max(0, min(LOADS, 2 * LPI) - AHEAD)
            if fresh:
                with sp.Fori(0, fresh) as c:
                    load(c + AHEAD, False)
                    stores(c)
            if LOADS > 2 * LPI:
                with sp.Fori(fresh, LOADS - AHEAD) as c:
                    load(c + AHEAD, True)
                    stores(c)
            with sp.Fori(max(0, LOADS - AHEAD), LOADS) as c:
                stores(c)
            for s in range(2):
                sp.wait_ge(s_st[s], 16 * (NG // 2))
            if scratch:
                sp.wait_ge(s_fill, 16 * sum(pieces))

        @block.gpsimd
        def _(pool):
            pool.memset(b_row[:], 0.0).then_inc(s_zero, 1)
            pool.memset(b_col[:], 0.0).then_inc(s_zero, 1)
            pool.memset(zeros[:], 0.0).then_inc(s_zero, 1)

            def add_x(q):
                pool.wait_ge(s_ld, q // CH * 16 + 16)
                wait(pool, s_ax, q)
                pool.tensor_tensor(acc_x[:], acc_x[:], ring[:, slot(q), :], ALU.add).then_inc(s_ax, 1)

            def boundary(n):
                pool.wait_ge(s_az, 2 * n + 4)
                pool.wait_ge(s_stat, n + 1)
                pool.sem_inc(s_pass, 1)
                state["n"] = n

            def lead(k, s, stats_too):
                g, on = gated(k, 0)
                if on:
                    wait(pool, s_xl, g - 1)
                    if not isinstance(g, int):
                        pool.sem_inc(s_pass, 1)
                    st = stats[:, bass.ds(state["n"] % 2, 1)]
                    pool.tensor_tensor(xn[:, s], ring[:, slot(g), :],
                                       st[:, :, 0:1, :].rearrange("p a b w -> p (a b) w").broadcast_to([P, JG, W]),
                                       ALU.subtract).then_inc(s_xc, 1)
                    pool.wait_ge(s_xc, g + 1)
                    if not isinstance(g, int):
                        pool.sem_inc(s_pass, 1)
                    pool.tensor_tensor(xn[:, s], xn[:, s],
                                       st[:, :, 1:2, :].rearrange("p a b w -> p (a b) w").broadcast_to([P, JG, W]),
                                       ALU.mult).then_inc(s_xn, 1)
                if on and stats_too:
                    add_x(g + G)
                g, on = gated(k, 2)
                if on:
                    pool.wait_ge(s_zh, g + 1)
                    wait(pool, s_wmm, g - 1)
                    pool.tensor_tensor(ZD[1][:, s].rearrange("p a b -> p (a b)"), zk[:, s],
                                       ZD[0][:, s].rearrange("p a b -> p (a b)"), ALU.subtract).then_inc(s_zl, 1)
                    for q in range(2):
                        if q:
                            pool.wait_ge(s_zl, g + 1)
                        src = ZD[q][:, s, 8:9, MAIN:UP]
                        pool.tensor_tensor(ZC[q][:, s], src.broadcast_to([P, CG, REM]),
                                           corner_mask.rearrange("p (c r) -> p c r", r=REM),
                                           ALU.mult).then_inc(s_zc, 1)

            state = {}
            pool.wait_ge(s_az, 2)
            with pool.Fori(0, G) as q:
                pool.wait_ge(s_ld, q // CH * 16 + 16)
                pool.wait_ge(s_ax, q)
                pool.tensor_tensor(acc_x[:], acc_x[:], ring[:, slot(q), :], ALU.add).then_inc(s_ax, 1)
            over_groups(pool, lead, boundary)

        @block.scalar
        def _(act):
            def square(q, s):
                act.wait_ge(s_ld, q // CH * 16 + 16)
                wait(act, s_asq, q - 1)
                act.activation(sq[:, s], ring[:, slot(q), :], ACT.Square).then_inc(s_sq, 1)

            def boundary(n):
                act.wait_ge(s_var, n + 1)
                act.activation(std[:], mom[:, 1, :], ACT.Sqrt).then_inc(s_std, 1)

            def lead(k, s, stats_too):
                o = 1 - s
                g, on = gated(k, 0)
                if on:
                    act.wait_ge(s_xn, g + 1)
                    wait(act, s_vmm, g - 1)
                    act.activation(XD[0][:, s], xn[:, s], ACT.Copy).then_inc(s_xh, 1)
                if on and stats_too:
                    square(g + G, s)
                g, on = gated(k, 1)
                if on:
                    act.wait_ge(s_vmm, g + 1)
                    wait(act, s_zmm, 3 * (g - 1))
                    act.activation(VD[0][:, o].rearrange("p i a -> p a i"), v_ps[:, :, 0:2 * VW],
                                   ACT.Copy).then_inc(s_vh, 1)
                g, on = gated(k, 2)
                if on:
                    for c in range(3):
                        act.wait_ge(s_zmm, 3 * g + c + 1)
                        wait(act, s_zk, 3 * (g - 1) + c + 1)
                        act.activation(zr[:, c], z_ps[:, c, 0:3 * UP], ACT.Relu, scale=0.2).then_inc(s_zr, 1)
                g, on = gated(k, 3)
                if on:
                    act.wait_ge(s_wmm, g + 1)
                    wait(act, s_omm, g - 1)
                    act.activation(WD[0][:, o], w_ps[:], ACT.Copy).then_inc(s_wh, 1)
                    act.activation(RD[0][:, o], r_ps[0:CG * REM, 0:H], ACT.Copy).then_inc(s_wh, 1)
                g, on = gated(k, 2)
                if on:
                    act.wait_ge(s_clip, g + 1)
                    wait(act, s_wmm, g - 1)
                    wait(act, s_zc, 2 * (g - 1))
                    act.activation(ZD[0][:, s].rearrange("p a b -> p (a b)"), zk[:, s], ACT.Copy).then_inc(s_zh, 1)
                    for q in range(2):
                        act.wait_ge((s_zh, s_zl)[q], g + 1)
                        act.activation(ZT[q][:, s], ZD[q][:, s, 0:CG, MAIN:UP], ACT.Copy).then_inc(s_zt, 1)

            with act.Fori(0, G // 2) as i:
                for s in range(2):
                    q = i * 2
                    act.wait_ge(s_ld, (q + s) // CH * 16 + 16)
                    act.wait_ge(s_asq, q + s)
                    act.activation(sq[:, s], ring[:, slot(q + s), :], ACT.Square).then_inc(s_sq, 1)
            over_groups(act, lead, boundary)

        @block.vector
        def _(dve):
            dve.memset(acc_x[:], 0.0).then_inc(s_az, 1)
            dve.memset(acc_sq[:], 0.0).then_inc(s_az, 1)
            scale = {"up_rows": 2.0, "up_cols": -2.0 * 2.0 ** 0.5, "down_main_neg": -1.0, "down_tail_cols": -1.0}
            for i, (k, n) in enumerate(shapes.items()):
                dve.wait_ge(s_const, 16 * (i + 1))
                dve.tensor_scalar(scaled[:, 0:n], stage[:, 0:n], scale.get(k, 1.0), None, ALU.mult).then_inc(s_cv, 1)
                dve.wait_ge(s_cv, 3 * i + 1)
                dve.tensor_copy(cw[k][0][:], scaled[:, 0:n]).then_inc(s_cv, 1)
                dve.wait_ge(s_cv, 3 * i + 2)
                if k == "average":
                    dve.tensor_copy(average[:], scaled[:, 0:n]).then_inc(s_cv, 1)
                else:
                    dve.tensor_tensor(cw[k][1][:], scaled[:, 0:n], cw[k][0][:], ALU.subtract).then_inc(s_cv, 1)
                dve.wait_ge(s_cv, 3 * i + 3)
            n = 3 * len(shapes)
            dve.wait_ge(s_bias, 64)
            for src, dst in ((b_row, bias_row), (b_col, bias_col)):
                dve.tensor_scalar(src[:], src[:], -(2.0 ** 0.5), None, ALU.mult).then_inc(s_cv, 1)
                dve.wait_ge(s_cv, n + 1)
                dve.tensor_copy(dst[:], src[:]).then_inc(s_cv, 1)
                dve.wait_ge(s_cv, n + 2)
                dve.tensor_tensor(dst[32:64, :], src[32:64, :], dst[32:64, :], ALU.subtract).then_inc(s_cv, 1)
                n += 3

            def add_sq(q, s):
                dve.wait_ge(s_sq, q + 1)
                wait(dve, s_asq, q)
                dve.tensor_tensor(acc_sq[:], acc_sq[:], sq[:, s], ALU.add).then_inc(s_asq, 1)

            def boundary(n):
                dve.wait_ge(s_ax, n * G + G)
                dve.wait_ge(s_asq, n * G + G)
                dve.tensor_reduce(sums[:, 0, :], acc_x[:].rearrange("p j w -> p w j"), AX.X, ALU.add).then_inc(s_sum, 1)
                dve.tensor_reduce(sums[:, 1, :], acc_sq[:].rearrange("p j w -> p w j"), AX.X, ALU.add).then_inc(s_sum, 1)
                dve.wait_ge(s_sum, 2 * n + 2)
                dve.memset(acc_x[:], 0.0).then_inc(s_az, 1)
                dve.memset(acc_sq[:], 0.0).then_inc(s_az, 1)
                dve.wait_ge(s_mom, n + 1)
                if not isinstance(n, int) or n:
                    dve.wait_ge(s_xn, n * G)
                st = stats[:, bass.ds(n % 2, 1)].rearrange("p a b w -> p (a b) w")
                dve.tensor_copy(mom[:], o_ps[:, 256:256 + 2 * W].rearrange("p (a w) -> p a w", a=2)).then_inc(s_momr, 1)
                dve.wait_ge(s_momr, 4 * n + 1)
                dve.tensor_copy(st[:, 0:1, :], mom[:, 0:1, :]).then_inc(s_momr, 1)
                dve.tensor_tensor(mom[:, 0, :], mom[:, 0, :], mom[:, 0, :], ALU.mult).then_inc(s_momr, 1)
                dve.wait_ge(s_momr, 4 * n + 3)
                dve.tensor_tensor(mom[:, 1, :], mom[:, 1, :], mom[:, 0, :], ALU.subtract).then_inc(s_momr, 1)
                dve.wait_ge(s_momr, 4 * n + 4)
                dve.tensor_scalar(mom[:, 1, :], mom[:, 1, :], 0.0, LN_EPS, ALU.max, ALU.add).then_inc(s_var, 1)
                dve.wait_ge(s_std, n + 1)
                dve.reciprocal(st[:, 1:2, :], std[:].unsqueeze(1)).then_inc(s_stat, 1)

            def lead(k, s, stats_too):
                o = 1 - s
                g, on = gated(k, 0)
                if on:
                    dve.wait_ge(s_xh, g + 1)
                    wait(dve, s_vmm, g - 1)
                    dve.tensor_tensor(XD[1][:, s], xn[:, s], XD[0][:, s], ALU.subtract).then_inc(s_xl, 1)
                if on and stats_too:
                    add_sq(g + G, s)
                g, on = gated(k, 1)
                if on:
                    dve.wait_ge(s_vh, g + 1)
                    dve.tensor_tensor(VD[1][:, o].rearrange("p i a -> p a i"), v_ps[:, :, 0:2 * VW],
                                      VD[0][:, o].rearrange("p i a -> p a i"),
                                      ALU.subtract).then_inc(s_vl, 1)
                g, on = gated(k, 2)
                if on:
                    wait(dve, s_zl, g - 1)
                    for c in range(3):
                        dve.wait_ge(s_zr, 3 * g + c + 1)
                        dve.scalar_tensor_tensor(out=zk[:, s, c * 3 * UP:(c + 1) * 3 * UP], in0=z_ps[:, c, 0:3 * UP],
                                                 scalar=-CLAMP, in1=zr[:, c], op0=ALU.max,
                                                 op1=ALU.min).then_inc(s_zk, 1)
                    dve.wait_ge(s_zk, 3 * g + 3)
                    dve.tensor_scalar(zk[:, s], zk[:, s], CLAMP, None, ALU.min).then_inc(s_clip, 1)
                g, on = gated(k, 3)
                if on:
                    dve.wait_ge(s_wh, 2 * g + 1)
                    dve.tensor_tensor(WD[1][:, o], w_ps[:], WD[0][:, o], ALU.subtract).then_inc(s_wl, 1)
                    dve.wait_ge(s_wh, 2 * g + 2)
                    dve.tensor_tensor(RD[1][:, o], r_ps[0:CG * REM, 0:H], RD[0][:, o],
                                      ALU.subtract).then_inc(s_wl, 1)
                g, on = gated(k, 4)
                if on:
                    dve.wait_ge(s_omm, g + 1)
                    wait(dve, s_st[s], 8 * (g - s))
                    dve.tensor_tensor(ob[:, s], o_ps[:, 0:JG * W].rearrange("p (j w) -> p j w", j=JG),
                                      ring[:, slot(g), :], ALU.add).then_inc(s_ob, 1)

            dve.wait_ge(s_az, 2)
            with dve.Fori(0, G // 2) as i:
                for s in range(2):
                    q = i * 2
                    dve.wait_ge(s_sq, q + s + 1)
                    dve.wait_ge(s_asq, q + s)
                    dve.tensor_tensor(acc_sq[:], acc_sq[:], sq[:, s], ALU.add).then_inc(s_asq, 1)
            over_groups(dve, lead, boundary)

        @block.tensor
        def _(pe):
            def mm(dst, a, b, first=False):
                return pe.matmul(dst, a, b, start=first, stop=False, skip_group_check=True)

            def split(dst, a, b, first=False):
                mm(dst, a[0], b[0], first)
                mm(dst, a[0], b[1])
                return mm(dst, a[1], b[0])

            def rows_up(g, s):
                pe.wait_ge(s_xl, g + 1)
                wait(pe, s_vl, g)
                for jp in range(2):
                    m = split(v_ps[:, jp, 0:2 * VW],
                              [t[:, s, 2 * jp:2 * jp + 2, :].rearrange("p j w -> p (j w)") for t in XD], up1, True)
                m.then_inc(s_vmm, 1)

            def cols_up(g, s):
                pe.wait_ge(s_vl, g + 1)
                for c in range(3):
                    wait(pe, s_zk, 3 * (g - 1) + c + 1)
                    nmain = min(3, CG - 3 * c)
                    pe.matmul(z_ps[:, c, 0:nmain * UP], ones_rows,
                              bias_row[:, bass.ds((g % G) * CG + 3 * c, nmain)].unsqueeze(2).broadcast_to([P, nmain, UP]),
                              start=True, stop=False, skip_group_check=True)
                    for i in range(nmain):
                        ch = 3 * c + i
                        jp, jj, cp = ch // 4, ch // 2 % 2, ch % 2
                        m = split(z_ps[:, c, i * UP:(i + 1) * UP], [t[:, s, cp * MAIN:(cp + 1) * MAIN, jp] for t in VD],
                                  [t[:, jj, :] for t in up2])
                    if c == 2:
                        mm(z_ps[:, c, 2 * UP:3 * UP], pick_rows,
                           bias_col[:, bass.ds(g % G, 1)].broadcast_to([P, UP]))
                        for jj in range(2):
                            m = split(z_ps[64 * jj:64 * jj + 64, c, 2 * UP:3 * UP],
                                      [t[:, s, 2 * MAIN:2 * VW, :].rearrange("p i a -> p (i a)") for t in VD],
                                      [t[:, jj, :] for t in up2])
                    m.then_inc(s_zmm, 1)

            def rows_down(g, s):
                pe.wait_ge(s_zc, 2 * g + 2)
                pe.wait_ge(s_zt, 2 * g + 2)
                wait(pe, s_wl, 2 * g)
                for ch in range(CG):
                    split(w_ps[:, ch * H:(ch + 1) * H], [t[:, s, ch, 0:MAIN] for t in ZD], dn3, ch == 0)
                split(w_ps[:].rearrange("p (c h) -> p c h", c=CG)[:, :, H - TAIL:H],
                      [t[:, s, CG, 0:MAIN] for t in ZD], dn3r)
                split(r_ps[0:CG * REM, 0:H], [t[:, s].rearrange("p c r -> p (c r)") for t in ZT], dn3, True)
                split(r_ps[0:CG * REM, H - TAIL:H],
                      [t[:, s].rearrange("p c r -> p (c r)") for t in ZC], dn3c).then_inc(s_wmm, 1)

            def cols_down(g, s):
                pe.wait_ge(s_wl, 2 * g + 2)
                wait(pe, s_ob, g)
                for j in range(JG):
                    split(o_ps[:, j * W:(j + 1) * W], [t[:, s, 2 * j * H:(2 * j + 2) * H] for t in WD], dn4, j == 0)
                ov = o_ps[:, 0:JG * W].rearrange("p (j w) -> p j w", j=JG)
                for cp in range(2):
                    m = split(ov[64 * cp:64 * cp + 64, :, W - TAIL:W], [t[:, s, :] for t in RD],
                              [t[0:CG * REM, cp, :] for t in dn4r])
                m.then_inc(s_omm, 1)

            def boundary(n):
                pe.wait_ge(s_sum, 2 * n + 2)
                if not isinstance(n, int) or n:
                    pe.wait_ge(s_ob, n * G - LAG)
                pe.matmul(o_ps[:, 256:256 + 2 * W], average[:], sums[:].rearrange("p a w -> p (a w)"),
                          start=True, stop=True, skip_group_check=True).then_inc(s_mom, 1)
                pe.wait_ge(s_var, n + 1)
                pe.sem_inc(s_pass, 1)

            def lead(k, s, stats_too):
                o = 1 - s
                for lag, step, par in ((1, rows_up, o), (2, cols_up, s), (4, cols_down, s), (3, rows_down, o)):
                    g, on = gated(k, lag)
                    if on:
                        step(g, par)

            pe.wait_ge(s_cv, 3 * len(shapes) + 6)
            over_groups(pe, lead, boundary)

def conv_layouts(up, down):
    u = np.zeros((UP, H), up.dtype)
    for t in range(TAPS):
        for h in range(H):
            u[2 * h + t, h] = up[t]
    d = np.zeros((H, UP), down.dtype)
    for t in range(TAPS):
        for h in range(H):
            d[h, 2 * h + t] = down[TAPS - 1 - t]
    ut, dt = u.T, d.T
    c = {}
    a = np.zeros((2, H, 2 * VW), up.dtype)
    b = np.zeros((2, W, 2, UP), up.dtype)
    for q in range(2):
        a[q, :, q * MAIN:(q + 1) * MAIN] = ut[:, :MAIN]
        a[q, :, 2 * MAIN + q * REMP:2 * MAIN + q * REMP + REM] = ut[:, MAIN:]
        b[q, :, q, :] = ut
    c["up_rows"] = a.reshape(P, -1)
    c["up_cols"] = b.reshape(P, -1)
    c["down_main"] = dt[:MAIN].copy()
    c["down_main_neg"] = dt[:MAIN].copy()
    blk = np.zeros((2, 2, REMP, 2, CG, TAIL), down.dtype)
    cor = np.zeros((2, 2, REMP, 2, TAIL), down.dtype)
    mask = np.zeros((2, 2, REMP, 2, CG, REM), np.float32)
    pick = np.zeros((P, 2, 2, REMP, 2), np.float32)
    for jj in range(2):
        for jp in range(2):
            for cp in range(2):
                ch = 4 * jp + 2 * jj + cp
                blk[jj, cp, :REM, jp, ch] = dt[MAIN:, H - TAIL:]
                cor[jj, cp, :REM, jp] = dt[MAIN:, H - TAIL:]
                mask[jj, cp, :, jp, ch] = 1
                pick[ch, jj, cp, :, jp] = 1
                pick[32 + ch, jj, cp, :, jp] = 1
    c["down_tail_block"] = blk.reshape(P, -1)
    c["down_tail_corner"] = cor.reshape(P, -1)
    cols = np.zeros((P, 2, JG, TAIL), down.dtype)
    for ch in range(CG):
        cols[ch * REM:(ch + 1) * REM, ch % 2, ch // 2] = dt[MAIN:, H - TAIL:]
    c["down_tail_cols"] = cols.reshape(P, -1)
    c["corner_mask"] = mask.reshape(P, -1)
    c["bias_pick"] = pick.reshape(P, -1)
    ones = np.zeros((P, P), np.float32)
    ones[0] = ones[32] = 1
    c["bias_ones"] = ones
    return c

def average_matrix(C):
    a = np.zeros((2, H, 2, H), np.float32)
    for h in range(H):
        a[:, h, :, h] = 1.0 / C
    return a.reshape(P, P)


TB = 4
TOK = TB * P
GROUPS, PICK_GROUPS, TOPK = 8, 4, 8
ROUTE_SCALE = 2.5
WSCALE = 64.0
CAP = 1024
BIG = 1e30
FAR = float(1 << 20)
LN_T_EPS = 1e-5

class Steps:

    def __init__(self, eng, sem):
        self.eng, self.sem, self.j, self.base = eng, sem, 0, 0

    def begin(self, index, per):
        self.base, self.j, self.per = index * per, 0, per

    def did(self, ins):
        ins.then_inc(self.sem, 1)
        self.j += 1
        return self.j

    def sync(self, settle=False):
        self.eng.wait_ge(self.sem, self.base + self.j)
        if settle:
            self.eng.sem_inc(self.passed, 1)

    def end(self):
        assert self.j == self.per, (self.j, self.per)

def route_phase(nc, out, gate_wt, gate_b, consts, xtok, xrows, slots, flags, executed):
    from contextlib import ExitStack
    U32, I32 = mybir.dt.uint32, mybir.dt.int32
    NI, C = out.shape[0], out.shape[1]
    PIX = out.shape[2] * out.shape[3]
    T = NI * PIX
    KC = C // P
    E = gate_wt.shape[1]
    EG = E // GROUPS
    NB = T // TOK
    BPI = PIX // TOK
    ROW = xrows.shape[1]
    out_v = out.rearrange("n (k p) h w -> n p k (h w)", p=P)
    with ExitStack() as ctx:
        def sb(name, shape, dt=F32):
            return ctx.enter_context(nc.sbuf_tensor("r_" + name, shape, dt))

        def ps(name, shape):
            return ctx.enter_context(nc.psum_tensor("r_" + name, shape, F32))

        def sem(name):
            return ctx.enter_context(nc.semaphore("r_" + name))

        xs = sb("xs", [P, 2, KC, TOK])
        xt = sb("xt", [P, 2, TB, C])
        xn = sb("xn", [P, TB, C])
        rows = sb("rows", [P, 2, TB, ROW])
        gw = sb("gw", [P, KC, E])
        gb = sb("gb", [P, E])
        gsum = sb("gsum", [P, E])
        tri16 = sb("tri16", [P, 2, P], F16)
        st6, mv = sb("st6", [P, TB, 6]), sb("mv", [P, TB, 2])
        ve, sd, rstd, nrstd = (sb(n, [P, TB]) for n in ("ve", "sd", "rstd", "nrstd"))
        lg, sc, sg, sm = (sb(n, [P, TB, E]) for n in ("lg", "sc", "sg", "sm"))
        srt = sb("srt", [P, TB, GROUPS, 8])
        g12, mr = sb("g12", [P, TB, 12]), sb("mr", [P, TB, 12])
        v8g, r8 = sb("v8g", [P, TB, 8]), sb("r8", [P, TB, 8])
        pen = sb("pen", [P, TB, GROUPS])
        v8e, mre = sb("v8e", [P, TB, 8]), sb("mre", [P, TB, E])
        mk, mk16 = sb("mk", [P, TB, E]), sb("mk16", [P, TB, E], F16)
        base, limit = sb("base", [P, E]), sb("limit", [P, E])
        pos, over, slot = (sb(n, [P, TB, E]) for n in ("pos", "over", "slot"))
        t8 = sb("t8", [P, TB, 8])
        idx = sb("idx", [P, 2, TB, 8], U32)
        wsel, wsum, winv = sb("wsel", [P, TB, E]), sb("wsum", [P, TB]), sb("winv", [P, TB])
        tid, tid_u = sb("tid", [P, TB]), sb("tid_u", [P, 2, TB], U32)
        gap, gmin = sb("gap", [P, E]), sb("gmin", [P, 1])
        consts_f = sb("consts", [P, consts.shape[1]])
        first_slot, first_tok = consts_f[:, 3 * P:3 * P + E], consts_f[:, 3 * P + E:3 * P + E + TB]
        empty_f = consts_f[:, 3 * P + E + TB:]
        init_ids = sb("init_ids", [P, E * CAP // P], U32)

        t_ps = ps("t_ps", [P, TB, C])
        g_ps = ps("g_ps", [P, 512])
        p_ps = ps("p_ps", [P, 512])
        c_ps = ps("c_ps", [P, 512])

        s_in, s_prep, s_init, s_gs = sem("inputs"), sem("prepared"), sem("initialised"), sem("gate_sums")
        s_ii, s_dd = sem("cleared"), sem("dve_steps")
        s_ld = [sem("loaded0"), sem("loaded1")]
        s_t, s_p = sem("turned"), sem("counted")
        s_xt, s_sd, s_xh, s_sg = sem("xt_copied"), sem("std"), sem("x_hi"), sem("scores")
        s_flag, s_pass = sem("flag_set"), sem("pass")
        s_stx, s_str = [sem("xt_stored0"), sem("xt_stored1")], [sem("rows_stored0"), sem("rows_stored1")]
        s_sc = [sem("ids_scattered0"), sem("ids_scattered1")]
        DSTEPS = 97
        at = {}

        phase = ExitStack()
        block = phase.enter_context(nc.Block())

        def hi_part(s):
            return rows[:, s, :, 0:C // 2].bitcast(F16)

        def lo_part(s):
            return rows[:, s, :, C // 2:C].bitcast(F16)

        def batches(eng, body):
            eng.wait_ge(s_prep, 6)
            with eng.Fori(0, NB // 2) as i:
                for s in range(2):
                    b = i * 2 + s
                    go = eng.value_load(flags[0:1, bass.ds(b, 1)], min_val=0, max_val=1)
                    with eng.If(go):
                        body(b, s)
                        eng.wait_ge(s_flag, b)
                        eng.sem_inc(s_pass, 1)

        @block.vector
        def _(dve):
            dve.memset(flags[:], 0).then_inc(s_ii, 1)
            dve.memset(executed[:], 0).then_inc(s_ii, 1)
            dve.memset(g12[:], -BIG).then_inc(s_prep, 1)
            dve.memset(r8[:], -BIG).then_inc(s_prep, 1)
            dve.wait_ge(s_in, 48)
            dve.tensor_copy(tri16[:].rearrange("p a q -> p (a q)"), consts_f[:, 0:2 * P]).then_inc(s_gs, 1)
            dve.tensor_copy(init_ids[:], empty_f).then_inc(s_ii, 1)
            dve.tensor_copy(tid[:], first_tok).then_inc(s_prep, 1)
            dve.tensor_copy(base[:], first_slot).then_inc(s_prep, 1)
            dve.tensor_scalar(limit[:], first_slot, float(CAP), None, ALU.add).then_inc(s_prep, 1)
            dve.wait_ge(s_gs, 2)
            dve.tensor_copy(gsum[:], g_ps[:, 0:E]).then_inc(s_gs, 1)
            dve.wait_ge(s_ii, 3)
            dve.wait_ge(s_gs, 3)
            dve.memset(flags[0:1, 0:2], 1).then_inc(s_prep, 1)

            def body(b, s):
                d = Steps(dve, s_dd)
                d.passed = s_pass
                d.begin(b, DSTEPS)
                dve.wait_ge(s_ii, b + 3)
                dve.wait_ge(s_xt, b + 1)
                for i in range(TB):
                    d.did(dve.bn_stats(st6[:, i], xt[:, s, i]))
                d.sync(settle=True)
                for i in range(TB):
                    d.did(dve.bn_aggr(mv[:, i], st6[:, i]))
                d.sync()
                at["ve"] = d.did(dve.tensor_scalar(ve[:], mv[:, :, 1], LN_T_EPS, None, ALU.add))
                dve.wait_ge(s_sd, b + 1)
                d.did(dve.reciprocal(rstd[:], sd[:]))
                d.sync()
                dve.wait_ge(s_xh, b)
                for i in range(TB):
                    at["xn"] = d.did(dve.tensor_scalar(xn[:, i], xt[:, s, i], mv[:, i, 0:1], rstd[:, i:i + 1],
                                                       ALU.subtract, ALU.mult))
                d.did(dve.tensor_scalar(nrstd[:], rstd[:], -1.0, None, ALU.mult))
                for i in range(TB):
                    at["lg"] = d.did(dve.scalar_tensor_tensor(
                        out=lg[:, i], in0=gsum[:], scalar=mv[:, i, 0:1], in1=g_ps[:, i * E:(i + 1) * E],
                        op0=ALU.mult, op1=ALU.subtract))
                dve.wait_ge(s_xh, b + 1)
                d.did(dve.tensor_tensor(lo_part(s), xn[:], hi_part(s), ALU.subtract))
                dve.wait_ge(s_sg, b + 1)
                d.did(dve.tensor_tensor(sg[:], sc[:], gb[:].unsqueeze(1).broadcast_to([P, TB, E]), ALU.add))
                d.sync(settle=True)
                for i in range(TB):
                    for g in range(GROUPS):
                        d.did(dve.max(srt[:, i, g], sg[:, i, g * EG:(g + 1) * EG]))
                d.sync()
                d.did(dve.tensor_tensor(g12[:, :, 0:GROUPS], srt[:, :, :, 0], srt[:, :, :, 1], ALU.add))
                d.sync(settle=True)
                for i in range(TB):
                    d.did(dve.max(v8g[:, i], g12[:, i, 0:GROUPS]))
                d.sync()
                d.did(dve.tensor_copy(r8[:, :, 0:PICK_GROUPS], v8g[:, :, 0:PICK_GROUPS]))
                d.sync(settle=True)
                for i in range(TB):
                    d.did(dve.match_replace(mr[:, i], r8[:, i], g12[:, i], BIG))
                d.sync()
                d.did(dve.tensor_scalar(pen[:], mr[:, :, 0:GROUPS], BIG / 2, BIG, ALU.is_ge, ALU.mult))
                d.sync()
                d.did(dve.tensor_scalar(pen[:], pen[:], BIG, None, ALU.subtract))
                d.sync()
                d.did(dve.tensor_tensor(sm[:].rearrange("p i (g e) -> p (i g) e", g=GROUPS),
                                        sg[:].rearrange("p i (g e) -> p (i g) e", g=GROUPS),
                                        pen[:].rearrange("p i g -> p (i g)").unsqueeze(2).broadcast_to([P, TB * GROUPS, EG]),
                                        ALU.add))
                d.sync(settle=True)
                for i in range(TB):
                    d.did(dve.max(v8e[:, i], sm[:, i]))
                d.sync(settle=True)
                for i in range(TB):
                    d.did(dve.match_replace(mre[:, i], v8e[:, i], sm[:, i], -2 * BIG))
                d.sync()
                at["mk"] = d.did(dve.tensor_scalar(mk16[:], mre[:], -1.5 * BIG, None, ALU.is_lt))
                d.did(dve.tensor_scalar(mk[:], mre[:], -1.5 * BIG, None, ALU.is_lt))
                d.sync()
                d.did(dve.tensor_tensor(wsel[:], sc[:], mk[:], ALU.mult))
                d.sync()
                d.did(dve.tensor_reduce(wsum[:], wsel[:], AX.X, ALU.add))
                d.sync()
                d.did(dve.reciprocal(winv[:], wsum[:]))
                d.sync()
                for i in range(TB):
                    at["weights"] = d.did(dve.tensor_scalar(rows[:, s, i, C:C + E], wsel[:, i],
                                            winv[:, i:i + 1], ROUTE_SCALE / WSCALE, ALU.mult, ALU.mult))
                dve.wait_ge(s_p, b + 1)
                d.did(dve.tensor_tensor(pos[:], p_ps[:, 0:TB * E].rearrange("p (i e) -> p i e", i=TB),
                                        base[:].unsqueeze(1).broadcast_to([P, TB, E]), ALU.add))
                d.sync()
                at["base"] = d.did(dve.tensor_tensor(base[:], base[:], c_ps[:, 0:E], ALU.add))
                d.did(dve.tensor_tensor(over[:], pos[:], limit[:].unsqueeze(1).broadcast_to([P, TB, E]), ALU.is_ge))
                d.sync()
                d.did(dve.scalar_tensor_tensor(out=slot[:], in0=over[:], scalar=FAR, in1=pos[:],
                                               op0=ALU.mult, op1=ALU.add))
                d.did(dve.tensor_tensor(gap[:], base[:], limit[:], ALU.subtract))
                d.sync()
                d.did(dve.tensor_tensor(slot[:], slot[:], mk[:], ALU.mult))
                d.did(dve.tensor_reduce(gmin[:], gap[:], AX.X, ALU.min))
                d.sync(settle=True)
                for i in range(TB):
                    d.did(dve.max(t8[:, i], slot[:, i]))
                dve.tensor_scalar(executed[:], executed[:], 1.0, None, ALU.add).then_inc(s_ii, 1)
                dve.wait_ge(s_flag, b)
                dve.sem_inc(s_pass, 1)
                more = dve.value_load(flags[0:1, bass.ds(b + 1, 1)], min_val=0, max_val=1)
                with dve.If(more):
                    dve.tensor_scalar(flags[0:1, bass.ds(b + 2, 1)], gmin[0:1, :], 0.0, None,
                                      ALU.is_lt).then_inc(s_flag, 1)
                d.sync()
                dve.wait_ge(s_sc[s], (b - s) * (8 * TB * TOPK))
                d.did(dve.tensor_scalar(idx[:, s], t8[:], -1.0, None, ALU.add))
                at["done"] = d.did(dve.tensor_copy(tid_u[:, s], tid[:]))
                d.sync()
                d.did(dve.tensor_scalar(tid[:], tid[:], float(TOK), None, ALU.add))
                d.end()

            batches(dve, body)

        @block.sync
        def _(sp):
            sp.dma_start(gw[:], gate_wt.rearrange("(k p) e -> p k e", p=P)).then_inc(s_in, 16)
            sp.dma_start(gb[:], gate_b.rearrange("(a e) -> a e", a=1).broadcast_to([P, E])).then_inc(s_in, 16)
            sp.dma_start(consts_f[:], consts).then_inc(s_in, 16)
            sp.wait_ge(s_ii, 3)
            sp.dma_start(slots.rearrange("(p a) b -> p (a b)", p=P), init_ids[:]).then_inc(s_init, 16)
            sp.wait_ge(s_init, 16)

            def body(b, s):
                sp.wait_ge(s_t, b)
                sp.dma_start(xs[:, s], out_v[bass.ds(b // BPI, 1), :, :, bass.ds((b % BPI) * TOK, TOK)]
                             .rearrange("n p k t -> (n p) k t")).then_inc(s_ld[s], 16)
                sp.wait_ge(s_xt, b + 1)
                sp.dma_start(xtok[bass.ds(b * TOK, TOK), :].rearrange("(i p) c -> p i c", p=P),
                             xt[:, s]).then_inc(s_stx[s], 16)
                sp.wait_ge(s_dd, b * DSTEPS + at["weights"])
                sp.dma_start(xrows[bass.ds(b * TOK, TOK), :].rearrange("(i p) c -> p i c", p=P),
                             rows[:, s]).then_inc(s_str[s], 16)

            batches(sp, body)

        @block.gpsimd
        def _(pool):
            pool.wait_ge(s_init, 16)

            def body(b, s):
                pool.wait_ge(s_dd, b * DSTEPS + at["done"])
                pool.sem_inc(s_pass, 1)
                for i in range(TB):
                    for k in range(TOPK):
                        pool.indirect_dma_start(slots, bass.IndirectOffsetOnAxis(ap=idx[:, s, i, k:k + 1], axis=0),
                                                tid_u[:, s, i:i + 1], None, bounds_check=E * CAP - 1,
                                                oob_is_err=False).then_inc(s_sc[s], 16)

            batches(pool, body)

        @block.scalar
        def _(act):
            def body(b, s):
                act.wait_ge(s_t, b + 1)
                act.wait_ge(s_stx[s], (b - s) * 8)
                act.activation(xt[:, s], t_ps[:], ACT.Copy).then_inc(s_xt, 1)
                act.wait_ge(s_dd, b * DSTEPS + at["ve"])
                act.activation(sd[:], ve[:], ACT.Sqrt).then_inc(s_sd, 1)
                act.wait_ge(s_dd, b * DSTEPS + at["xn"])
                act.wait_ge(s_str[s], (b - s) * 8)
                act.activation(hi_part(s), xn[:], ACT.Copy).then_inc(s_xh, 1)
                act.wait_ge(s_dd, b * DSTEPS + at["lg"])
                for i in range(TB):
                    m = act.activation(sc[:, i], lg[:, i], ACT.Sigmoid, scale=nrstd[:, i:i + 1])
                m.then_inc(s_sg, 1)

            batches(act, body)

        @block.tensor
        def _(pe):
            ident, all_f = consts_f[:, 2 * P:3 * P], consts_f[:, P:2 * P]
            pe.wait_ge(s_in, 48)
            pe.wait_ge(s_gs, 1)
            for k in range(KC):
                m = pe.matmul(g_ps[:, 0:E], all_f, gw[:, k], start=k == 0, stop=k == KC - 1)
            m.then_inc(s_gs, 1)

            def body(b, s):
                pe.wait_ge(s_ld[s], (b - s) * 8 + 16)
                pe.wait_ge(s_xt, b)
                for i in range(TB):
                    for k in range(KC):
                        pe.transpose(t_ps[:, i, k * P:(k + 1) * P], xs[:, s, k, i * P:(i + 1) * P], ident)
                    for k in range(KC):
                        m = pe.matmul(g_ps[:, i * E:(i + 1) * E], xs[:, s, k, i * P:(i + 1) * P], gw[:, k],
                                      start=k == 0, stop=k == KC - 1, skip_group_check=True)
                m.then_inc(s_t, 1)
                pe.wait_ge(s_dd, b * DSTEPS + at["mk"])
                for i in range(TB):
                    for j in range(i + 1):
                        pe.matmul(p_ps[:, i * E:(i + 1) * E], tri16[:, 0 if j == i else 1], mk16[:, j],
                                  start=j == 0, stop=j == i, skip_group_check=True)
                for j in range(TB):
                    m = pe.matmul(c_ps[:, 0:E], tri16[:, 1], mk16[:, j], start=j == 0, stop=j == TB - 1)
                m.then_inc(s_p, 1)

            batches(pe, body)

        phase.close()
        block2 = ctx.enter_context(nc.Block())

        @block2.sync
        def _(sp):
            n = sp.value_load(executed[:], min_val=2, max_val=NB)
            for s in range(2):
                sp.wait_ge(s_stx[s], ((n + 1 - s) // 2) * 16)
                sp.wait_ge(s_str[s], ((n + 1 - s) // 2) * 16)
            sp.sem_inc(s_pass, 1)

        @block2.gpsimd
        def _(pool):
            n = pool.value_load(executed[:], min_val=2, max_val=NB)
            for s in range(2):
                pool.wait_ge(s_sc[s], ((n + 1 - s) // 2) * (16 * TB * TOPK))
            pool.sem_inc(s_pass, 1)

def route_consts(T, E):
    p = np.arange(P)
    before = (p[:, None] < p[None, :]).astype(np.float32)
    n = E * CAP // P
    empty = T + (p[:, None] * n + np.arange(n)[None, :]) % CAP
    return np.concatenate([
        before, np.ones((P, P), np.float32), np.eye(P, dtype=np.float32),
        np.broadcast_to(np.arange(E) * CAP + 1.0, (P, E)).astype(np.float32),
        (p[:, None] + P * np.arange(TB)[None, :]).astype(np.float32),
        empty.astype(np.float32)], axis=1)


def expert_phase(nc, w1, w3, w2, ident, slots, xrows, xtok):
    from contextlib import ExitStack
    U32 = mybir.dt.uint32
    E, C, M = w1.shape
    KC, MC = C // P, M // P
    ROW = xrows.shape[1]
    NT = CAP // P
    HALF = 512
    NH = CAP // HALF
    TH = HALF // P
    UNITS = NH * MC
    with ExitStack() as ctx:
        def sb(name, shape, dt=F32):
            return ctx.enter_context(nc.sbuf_tensor("e_" + name, shape, dt))

        def ps(name, shape):
            return ctx.enter_context(nc.psum_tensor("e_" + name, shape, F32))

        def sem(name):
            return ctx.enter_context(nc.semaphore("e_" + name))

        ident_f = sb("ident_f", [P, P])
        ident16 = sb("ident16", [P, P], F16)
        ids = sb("ids", [P, E, NT], U32)
        gather_ids = sb("gather_ids", [P, 2, NT], U32)
        scatter_ids = sb("scatter_ids", [P, 2, NT], U32)
        rows = sb("rows", [P, 2, NT, ROW])
        wcol = sb("weight_cols", [P, 2, NT])
        xt = [sb(f"xt_{q}", [P, 2, KC, CAP], F16) for q in ("hi", "lo")]
        wf = [sb(f"{n}_f", [P, KC, M]) for n in ("w1", "w3")] + [sb("w2_f", [P, MC, C])]
        wh = [[sb(f"{n}_{q}", [P, 2, C * M // P], F16) for q in ("hi", "lo")] for n in ("w1", "w3", "w2")]
        silu = sb("silu", [P, 2, HALF])
        hf = sb("h", [P, 2, HALF])
        h16 = [sb(f"h_{q}", [P, 2, MC, CAP], F16) for q in ("hi", "lo")]
        yb = sb("y", [P, 2, NT, C])

        x_ps = ps("x_ps", [P, 2, 512])
        h_ps = ps("h_ps", [P, 2, 2, 512])
        y_ps = ps("y_ps", [P, 2, 512])

        s_in, s_cv = sem("inputs"), sem("ident_ready")
        s_w, s_whi, s_wlo = [sem(f"w_loaded{j}") for j in range(3)], sem("w_hi"), sem("w_lo")
        s_gi, s_g = sem("gather_ids_ready"), [sem("gathered0"), sem("gathered1")]
        s_si, s_sc = sem("scatter_ids_ready"), [sem("scattered0"), sem("scattered1")]
        s_xmm, s_xhi, s_xlo, s_wc = sem("x_turned"), sem("xt_hi"), sem("xt_lo"), sem("weight_cols_ready")
        s_hmm, s_silu, s_hf, s_hhi, s_hlo = (sem("h_mm"), sem("silu_done"), sem("h_ready"), sem("h_hi"),
                                             sem("h_lo"))
        s_ymm, s_ye, s_yo, s_pass = sem("y_mm"), sem("y_even"), sem("y_odd"), sem("pass")

        def wait(eng, s, v):
            if not (isinstance(v, int) and v <= 0):
                eng.wait_ge(s, v)

        def over_experts(eng, step):
            for e in range(2):
                step(e, e % 2)
            with eng.Fori(1, E // 2 - 1) as i:
                for s in range(2):
                    step(i * 2 + s, s)
            for e in range(E - 2, E):
                step(e, e % 2)

        def exists(e):
            return not isinstance(e, int) or e < E

        block = ctx.enter_context(nc.Block())

        @block.sync
        def _(sp):
            sp.dma_start(ident_f[:], ident).then_inc(s_in, 16)
            sp.dma_start(ids[:], slots.rearrange("(e p t) a -> p e (t a)", p=P, t=NT)).then_inc(s_in, 16)
            weights = (w1, w3, w2)

            def load(e):
                for j in range(3):
                    if not isinstance(e, int) or e:
                        sp.wait_ge(s_wlo, 3 * (e - 1) + j + 1)
                    sp.dma_start(wf[j][:], weights[j][bass.ds(e, 1)].rearrange("e (k p) m -> (e p) k m", p=P)
                                 ).then_inc(s_w[j], 16)

            load(0)

            def step(e, s):
                if exists(e + 1):
                    load(e + 1)

            over_experts(sp, step)

        @block.gpsimd
        def _(pool):
            def gather(e, s):
                if not isinstance(e, int) or e >= 2:
                    pool.wait_ge(s_g[s], (e - s) * (8 * NT))
                pool.tensor_copy(gather_ids[:, s], ids[:, bass.ds(e, 1)].rearrange("p e t -> p (e t)")
                                 ).then_inc(s_gi, 1)
                if not isinstance(e, int) or e >= 2:
                    pool.wait_ge(s_xmm, (e - 1) * (2 * KC * NH))
                    pool.wait_ge(s_wc, e - 1)
                pool.wait_ge(s_gi, e + 1)
                pool.sem_inc(s_pass, 1)
                for t in range(NT):
                    pool.indirect_dma_start(rows[:, s, t], None, xrows,
                                            bass.IndirectOffsetOnAxis(ap=gather_ids[:, s, t:t + 1], axis=0)
                                            ).then_inc(s_g[s], 16)

            pool.wait_ge(s_in, 32)
            for e in range(2):
                gather(e, e)

            def step(e, s):
                if exists(e + 2):
                    gather(e + 2, s)
                wait(pool, s_sc[s], (e - s) * (8 * NT))
                pool.tensor_copy(scatter_ids[:, s], ids[:, bass.ds(e, 1)].rearrange("p e t -> p (e t)")
                                 ).then_inc(s_si, 1)
                pool.wait_ge(s_si, e + 1)
                wait(pool, s_sc[1 - s], (e + s) * (8 * NT))
                for t in range(NT):
                    pool.wait_ge((s_ye, s_yo)[t % 2], e * (NT // 2) + t // 2 + 1)
                    pool.sem_inc(s_pass, 1)
                    pool.indirect_dma_start(xtok, bass.IndirectOffsetOnAxis(ap=scatter_ids[:, s, t:t + 1], axis=0),
                                            yb[:, s, t], None, compute_op=ALU.add).then_inc(s_sc[s], 16)

            over_experts(pool, step)
            for s in range(2):
                pool.wait_ge(s_sc[s], (E // 2) * (16 * NT))

        @block.scalar
        def _(act):
            def w_hi(e, s, j):
                act.wait_ge(s_w[j], e * 16 + 16)
                if not isinstance(e, int) or e >= 2:
                    if j < 2:
                        act.wait_ge(s_hmm, (e - 1) * (2 * UNITS))
                    else:
                        act.wait_ge(s_ymm, (e - 1) * NT)
                act.activation(wh[j][0][:, s], wf[j][:].rearrange("p k m -> p (k m)"), ACT.Copy,
                               scale=WSCALE).then_inc(s_whi, 1)

            def x_hi(e, s, n):
                act.wait_ge(s_xmm, e * (2 * KC * NH) + 2 * n + 1)
                if not isinstance(e, int) or e >= 2:
                    act.wait_ge(s_hmm, (e - 1) * (2 * UNITS))
                act.activation(xt[0][:, s, n % KC, n // KC * HALF:(n // KC + 1) * HALF], x_ps[:, 0],
                               ACT.Copy).then_inc(s_xhi, 1)

            def step(e, s):
                o = 1 - s
                for u in range(UNITS):
                    act.wait_ge(s_hmm, e * (2 * UNITS) + 2 * u + 1)
                    wait(act, s_hf, e * UNITS + u - 1)
                    act.activation(silu[:, u % 2], h_ps[:, u % 2, 0], ACT.Silu, scale=1 / WSCALE).then_inc(s_silu, 1)
                    if exists(e + 1):
                        x_hi(e + 1, o, 2 * u)
                        x_hi(e + 1, o, 2 * u + 1)
                    act.wait_ge(s_hf, e * UNITS + u + 1)
                    wait(act, s_ymm, (e - 1) * NT)
                    act.activation(h16[0][:, s, u % MC, u // MC * HALF:(u // MC + 1) * HALF], hf[:, u % 2],
                                   ACT.Copy).then_inc(s_hhi, 1)
                    if exists(e + 1) and u < 3:
                        w_hi(e + 1, o, u)
                act.wait_ge(s_wc, e + 1)
                wait(act, s_sc[s], (e - s) * (8 * NT))
                for t in range(0, NT, 2):
                    act.wait_ge(s_ymm, e * NT + t + 1)
                    act.activation(yb[:, s, t], y_ps[:, 0], ACT.Copy, scale=wcol[:, s, t:t + 1]).then_inc(s_ye, 1)

            for j in range(3):
                w_hi(0, 0, j)
            for n in range(KC * NH):
                x_hi(0, 0, n)
            over_experts(act, step)

        @block.vector
        def _(dve):
            def w_lo(e, s, j):
                dve.wait_ge(s_whi, 3 * e + j + 1)
                dve.scalar_tensor_tensor(out=wh[j][1][:, s], in0=wf[j][:].rearrange("p k m -> p (k m)"),
                                         scalar=WSCALE, in1=wh[j][0][:, s], op0=ALU.mult,
                                         op1=ALU.subtract).then_inc(s_wlo, 1)

            def x_lo(e, s, n):
                dve.wait_ge(s_xmm, e * (2 * KC * NH) + 2 * n + 2)
                if not isinstance(e, int) or e >= 2:
                    dve.wait_ge(s_hmm, (e - 1) * (2 * UNITS))
                dve.tensor_copy(xt[1][:, s, n % KC, n // KC * HALF:(n // KC + 1) * HALF], x_ps[:, 1]).then_inc(s_xlo, 1)

            def weight_col(e, s):
                dve.wait_ge(s_g[s], (e - s) * (8 * NT) + 16 * NT)
                if not isinstance(e, int) or e >= 2:
                    dve.wait_ge(s_ye, (e - 1) * (NT // 2))
                    dve.wait_ge(s_yo, (e - 1) * (NT // 2))
                dve.tensor_copy(wcol[:, s].unsqueeze(2), rows[:, s, :, bass.ds(e + C, 1)]).then_inc(s_wc, 1)

            def step(e, s):
                o = 1 - s
                if exists(e + 1):
                    weight_col(e + 1, o)
                for u in range(UNITS):
                    dve.wait_ge(s_silu, e * UNITS + u + 1)
                    dve.wait_ge(s_hmm, e * (2 * UNITS) + 2 * u + 2)
                    wait(dve, s_hlo, e * UNITS + u - 1)
                    dve.scalar_tensor_tensor(out=hf[:, u % 2], in0=h_ps[:, u % 2, 1], scalar=1 / WSCALE,
                                             in1=silu[:, u % 2], op0=ALU.mult, op1=ALU.mult).then_inc(s_hf, 1)
                    if exists(e + 1):
                        x_lo(e + 1, o, 2 * u)
                        x_lo(e + 1, o, 2 * u + 1)
                    dve.wait_ge(s_hhi, e * UNITS + u + 1)
                    half = slice(u // MC * HALF, (u // MC + 1) * HALF)
                    dve.tensor_tensor(h16[1][:, s, u % MC, half], hf[:, u % 2], h16[0][:, s, u % MC, half],
                                      ALU.subtract).then_inc(s_hlo, 1)
                    if exists(e + 1) and u < 3:
                        w_lo(e + 1, o, u)
                wait(dve, s_sc[s], (e - s) * (8 * NT))
                dve.wait_ge(s_wc, e + 1)
                for t in range(1, NT, 2):
                    dve.wait_ge(s_ymm, e * NT + t + 1)
                    dve.tensor_scalar(yb[:, s, t], y_ps[:, 1], wcol[:, s, t:t + 1], None, ALU.mult).then_inc(s_yo, 1)

            dve.wait_ge(s_in, 32)
            dve.tensor_copy(ident16[:], ident_f[:]).then_inc(s_cv, 1)
            for j in range(3):
                w_lo(0, 0, j)
            weight_col(0, 0)
            for n in range(KC * NH):
                x_lo(0, 0, n)
            over_experts(dve, step)

        @block.tensor
        def _(pe):
            def mm(dst, a, b, first=False, last=False):
                return pe.matmul(dst, a, b, start=first, stop=last, skip_group_check=True)

            def turn(e, s, n):
                half, k = n // KC, n % KC
                for q in range(2):
                    wait(pe, (s_xhi, s_xlo)[q], e * (KC * NH) + n)
                    for t in range(TH):
                        words = rows[:, s, half * TH + t, q * (C // 2):(q + 1) * (C // 2)].bitcast(F16)
                        m = mm(x_ps[:, q, t * P:(t + 1) * P], words[:, k * P:(k + 1) * P], ident16[:],
                               t == 0, t == TH - 1)
                    m.then_inc(s_xmm, 1)

            def products(e, s, u, j):
                wait(pe, s_hf, e * UNITS + u - 1)
                half = slice(u // MC * HALF, (u // MC + 1) * HALF)
                for k in range(KC):
                    for a, b in ((0, 0), (0, 1), (1, 0)):
                        col = k * M + u % MC * P
                        m = mm(h_ps[:, u % 2, j], wh[j][a][:, s, col:col + P], xt[b][:, s, k, half],
                               k == 0 and a + b == 0, k == KC - 1 and a == 1)
                m.then_inc(s_hmm, 1)

            def step(e, s):
                o = 1 - s
                pe.wait_ge(s_wlo, 3 * e + 3)
                pe.wait_ge(s_xhi, (e + 1) * (KC * NH))
                pe.wait_ge(s_xlo, (e + 1) * (KC * NH))
                if exists(e + 1):
                    pe.wait_ge(s_g[o], (e + s) * (8 * NT) + 16 * NT)
                for u in range(UNITS):
                    for j in range(2):
                        products(e, s, u, j)
                        if exists(e + 1):
                            turn(e + 1, o, 2 * u + j)
                for t in range(NT):
                    if t % TH == 0:
                        pe.wait_ge(s_hlo, e * UNITS + (t // TH + 1) * MC)
                    wait(pe, (s_ye, s_yo)[t % 2], e * (NT // 2) + t // 2)
                    for mc in range(MC):
                        for a, b in ((0, 0), (0, 1), (1, 0)):
                            m = mm(y_ps[:, t % 2, 0:C], h16[a][:, s, mc, t * P:(t + 1) * P],
                                   wh[2][b][:, s, mc * C:(mc + 1) * C], mc == 0 and a + b == 0,
                                   mc == MC - 1 and a == 1)
                    m.then_inc(s_ymm, 1)

            pe.wait_ge(s_cv, 1)
            pe.wait_ge(s_g[0], 16 * NT)
            for n in range(KC * NH):
                turn(0, 0, n)
            over_experts(pe, step)


def finish_phase(nc, ident, xtok, flags, executed, out):
    from contextlib import ExitStack
    C = out.shape[1]
    KC = C // P
    PIX = out.shape[2] * out.shape[3]
    BPI = PIX // TOK
    NB = out.shape[0] * BPI
    out_v = out.rearrange("n (k p) h w -> n p k (h w)", p=P)
    with ExitStack() as ctx:
        def sem(name):
            return ctx.enter_context(nc.semaphore("f_" + name))

        ident_f = ctx.enter_context(nc.sbuf_tensor("f_ident", [P, P], F32))
        tok = ctx.enter_context(nc.sbuf_tensor("f_tokens", [P, 2, TB, C], F32))
        chan = ctx.enter_context(nc.sbuf_tensor("f_channels", [P, 2, KC, TOK], F32))
        t_ps = ctx.enter_context(nc.psum_tensor("f_t_ps", [P, 2, KC, TOK], F32))
        s_in, s_ld = sem("ident_loaded"), [sem("loaded0"), sem("loaded1")]
        s_t = [sem("turned0"), sem("turned1")]
        s_hi, s_lo = [sem("half1_copied0"), sem("half1_copied1")], [sem("half2_copied0"), sem("half2_copied1")]
        s_st, s_pass = [sem("stored0"), sem("stored1")], sem("pass")
        phase = ExitStack()
        block = phase.enter_context(nc.Block())

        def batches(eng, body):
            with eng.Fori(0, NB // 2) as i:
                for s in range(2):
                    b = i * 2 + s
                    go = eng.value_load(flags[0:1, bass.ds(b, 1)], min_val=0, max_val=1)
                    with eng.If(go):
                        body(i, b, s)

        def pixels(b):
            return out_v[bass.ds(b // BPI, 1), :, :, bass.ds((b % BPI) * TOK, TOK)].rearrange("n p k t -> (n p) k t")

        @block.sync
        def _(sp):
            sp.dma_start(ident_f[:], ident).then_inc(s_in, 16)

            def body(i, b, s):
                sp.wait_ge(s_t[s], i)
                sp.sem_inc(s_pass, 1)
                sp.dma_start(tok[:, s], xtok[bass.ds(b * TOK, TOK), :].rearrange("(i p) c -> p i c", p=P)
                             ).then_inc(s_ld[s], 16)

            batches(sp, body)

        @block.gpsimd
        def _(pool):
            def body(i, b, s):
                pool.wait_ge(s_hi[s], i + 1)
                pool.wait_ge(s_lo[s], i + 1)
                pool.dma_start(pixels(b), chan[:, s]).then_inc(s_st[s], 16)

            batches(pool, body)

        @block.tensor
        def _(pe):
            pe.wait_ge(s_in, 16)

            def body(i, b, s):
                pe.wait_ge(s_ld[s], i * 16 + 16)
                pe.wait_ge(s_hi[s], i)
                pe.wait_ge(s_lo[s], i)
                for k in range(KC):
                    for j in range(TB):
                        m = pe.transpose(t_ps[:, s, k, j * P:(j + 1) * P], tok[:, s, j, k * P:(k + 1) * P], ident_f[:])
                m.then_inc(s_t[s], 1)

            batches(pe, body)

        @block.scalar
        def _(act):
            def body(i, b, s):
                act.wait_ge(s_t[s], i + 1)
                act.wait_ge(s_st[s], i * 16)
                act.activation(chan[:, s, 0:KC // 2], t_ps[:, s, 0:KC // 2], ACT.Copy).then_inc(s_hi[s], 1)

            batches(act, body)

        @block.vector
        def _(dve):
            def body(i, b, s):
                dve.wait_ge(s_t[s], i + 1)
                dve.wait_ge(s_st[s], i * 16)
                dve.tensor_copy(chan[:, s, KC // 2:KC], t_ps[:, s, KC // 2:KC]).then_inc(s_lo[s], 1)

            batches(dve, body)

        phase.close()
        block2 = ctx.enter_context(nc.Block())

        @block2.sync
        def _(sp):
            n = sp.value_load(executed[:], min_val=2, max_val=NB)
            for s in range(2):
                sp.wait_ge(s_st[s], ((n + 1 - s) // 2) * 16)
            sp.sem_inc(s_pass, 1)


def metaformer(nc, x, bias, bias_cols, gate_wt, gate_b, w1, w3, w2, moe_consts, *rest):
    out = rest[-1]
    consts = dict(zip(CONV_CONSTS, rest[:-1]))
    NI, C = x.shape[0], x.shape[1]
    E = w1.shape[0]
    T = NI * x.shape[2] * x.shape[3]
    spare = CAP
    xtok = nc.dram_tensor("tokens", (T + spare, C), F32, kind="Internal").ap()
    xrows = nc.dram_tensor("normed_rows", (T + spare, C + E), F32, kind="Internal").ap()
    slots = nc.dram_tensor("slot_tokens", (E * CAP, 1), mybir.dt.uint32, kind="Internal").ap()
    ident = moe_consts[:, 2 * P:3 * P]
    with nc.sbuf_tensor("flags", [1, T // TOK + 2], mybir.dt.int32) as flags, \
            nc.sbuf_tensor("executed", [1, 1], mybir.dt.int32) as executed:
        conv_phase(nc, x, bias, bias_cols, consts, out, (xtok, xrows))
        route_phase(nc, out, gate_wt, gate_b, moe_consts, xtok, xrows, slots, flags, executed)
        expert_phase(nc, w1, w3, w2, ident, slots, xrows, xtok)
        finish_phase(nc, ident, xtok, flags, executed, out)

CONV_CONSTS = ("up_rows", "up_cols", "down_main", "down_main_neg", "down_tail_block", "down_tail_corner",
               "down_tail_cols", "corner_mask", "bias_pick", "bias_ones", "average")

def kernel(x, L0_conv_bias, L0_conv_up_filter, L0_conv_down_filter, L0_ffn_gate_w, L0_ffn_gate_b,
           L0_ffn_w1, L0_ffn_w3, L0_ffn_w2):
    import concourse.bacc as bacc
    from concourse.bass_utils import run_bass_kernel_spmd

    x, bias = np.asarray(x), np.asarray(L0_conv_bias)
    C = x.shape[1]
    T = x.shape[0] * x.shape[2] * x.shape[3]
    E = L0_ffn_gate_w.shape[0]
    conv = conv_layouts(np.asarray(L0_conv_up_filter), np.asarray(L0_conv_down_filter))
    conv["average"] = average_matrix(C)
    data = {"x": x, "bias": bias, "bias_cols": bias.reshape(-1, CG).T,
            "gate_wt": np.asarray(L0_ffn_gate_w).T, "gate_b": L0_ffn_gate_b,
            "w1": L0_ffn_w1, "w3": L0_ffn_w3, "w2": L0_ffn_w2, "moe_consts": route_consts(T, E)}
    data.update({f"conv_{k}": conv[k] for k in CONV_CONSTS})
    arrays = {f"{k}_dram": np.ascontiguousarray(v) for k, v in data.items()}
    nc = bacc.Bacc("TRN2", target_bir_lowering=False, num_devices=1)
    args = [nc.dram_tensor(k, v.shape, mybir.dt.from_np(v.dtype), kind="ExternalInput").ap()
            for k, v in arrays.items()]
    out = nc.dram_tensor("out_dram", x.shape, F32, kind="ExternalOutput").ap()
    metaformer(nc, *args, out)
    r = run_bass_kernel_spmd(nc, [arrays], core_ids=[0])
    return r.results[0]["out_dram"]
```
